# Optimizing a Trainium2 kernel written in Bass

```python
import numpy as np
import jax
import jax.numpy as jnp

def _softmax(x, axis=-1):
    return jax.nn.softmax(x, axis=axis)
def _gelu(x):
    return jax.nn.gelu(x, approximate=True)
def _silu(x):
    return jax.nn.silu(x)
def _sigmoid(x):
    return jax.nn.sigmoid(x)
def _layernorm(x, axis=-1, eps=1e-5):
    m = jnp.mean(x, axis=axis, keepdims=True)
    v = jnp.var(x, axis=axis, keepdims=True)
    return (x - m) / jnp.sqrt(v + eps)
def _scatter_add(tgt, idx, src, axis=0):
    return tgt.at[idx].add(src)
def _segment_sum(src, seg, n):
    return jax.ops.segment_sum(src, seg, n)

kernel_name = 'mk_rec_standalone_d1_rec_40f637'

def setup_inputs(seed: int = 0):
    np.random.seed(seed)
    _w = jnp.asarray
    def _rec_inputs():
        import jax
        import jax.numpy as jnp
        _rk = jax.random.key(seed)
        r_x = 7.22013e-05 + 1.00017 * jax.random.normal(jax.random.fold_in(_rk, 1), (4096, 512), jnp.float32)
        return r_x
    r_x = _rec_inputs()
    def _L0_rec_setup():
        import jax, jax.numpy as jnp
        import numpy as np
        IN, H1, H2, H3, H4, OUT = (512, 2048, 2048, 1024, 512, 1)
        key = jax.random.key(seed)
        ks = jax.random.split(key, 12)

        def lin(k, fan_in, fan_out):
            bound = 1.0 / np.sqrt(fan_in)
            k1, k2 = jax.random.split(k)
            W = jax.random.uniform(k1, (fan_out, fan_in), jnp.float32, -bound, bound)
            b = jax.random.uniform(k2, (fan_out,), jnp.float32, -bound, bound)
            return (W, b)
        x = jax.random.normal(ks[0], (16384, IN), jnp.float32)
        cross_w = jnp.ones((IN,), jnp.float32)
        cross_b = jnp.zeros((IN,), jnp.float32)
        W1, b1 = lin(ks[1], IN, H1)
        W2, b2 = lin(ks[2], H1, H2)
        W3, b3 = lin(ks[3], H2, H3)
        W4, b4 = lin(ks[4], H3, H4)
        Wo, bo = lin(ks[5], H4, OUT)
        return {'x': x, 'cross_w': cross_w, 'cross_b': cross_b, 'W1': W1, 'b1': b1, 'W2': W2, 'b2': b2, 'W3': W3, 'b3': b3, 'W4': W4, 'b4': b4, 'Wo': Wo, 'bo': bo}
    _L0_rec_all = _L0_rec_setup()
    _L0_rec_in = {k: v for k, v in _L0_rec_all.items() if k in ('cross_w', 'cross_b', 'W1', 'b1', 'W2', 'b2', 'W3', 'b3', 'W4', 'b4', 'Wo', 'bo', )}
    del _L0_rec_all

    return {
        "r_x": r_x,
        "L0_rec_cross_w": _L0_rec_in["cross_w"],
        "L0_rec_cross_b": _L0_rec_in["cross_b"],
        "L0_rec_W1": _L0_rec_in["W1"],
        "L0_rec_b1": _L0_rec_in["b1"],
        "L0_rec_W2": _L0_rec_in["W2"],
        "L0_rec_b2": _L0_rec_in["b2"],
        "L0_rec_W3": _L0_rec_in["W3"],
        "L0_rec_b3": _L0_rec_in["b3"],
        "L0_rec_W4": _L0_rec_in["W4"],
        "L0_rec_b4": _L0_rec_in["b4"],
        "L0_rec_Wo": _L0_rec_in["Wo"],
        "L0_rec_bo": _L0_rec_in["bo"],
    }

def reference(r_x, L0_rec_cross_w, L0_rec_cross_b, L0_rec_W1, L0_rec_b1, L0_rec_W2, L0_rec_b2, L0_rec_W3, L0_rec_b3, L0_rec_W4, L0_rec_b4, L0_rec_Wo, L0_rec_bo):
    import jax
    import jax.numpy as jnp
    def _L0_rec_ref(x, cross_w, cross_b, W1, b1, W2, b2, W3, b3, W4, b4, Wo, bo):
        import jax, jax.numpy as jnp
        import numpy as np
        IN, H1, H2, H3, H4, OUT = (512, 2048, 2048, 1024, 512, 1)
        xw = x @ cross_w
        h = x * xw[:, None] + cross_b + x
        h = jax.nn.relu(h @ W1.T + b1)
        h = jax.nn.relu(h @ W2.T + b2)
        h = jax.nn.relu(h @ W3.T + b3)
        h = jax.nn.relu(h @ W4.T + b4)
        return h @ Wo.T + bo

    y = _L0_rec_ref(r_x, L0_rec_cross_w, L0_rec_cross_b, L0_rec_W1, L0_rec_b1, L0_rec_W2, L0_rec_b2, L0_rec_W3, L0_rec_b3, L0_rec_W4, L0_rec_b4, L0_rec_Wo, L0_rec_bo)
    return y


_drawn_inputs = setup_inputs


def setup_inputs(seed=0):
    import zlib

    import numpy as np

    out = dict(_drawn_inputs(seed))
    spreads = {'L0_rec_cross_w': (1.0, 0.2), 'L0_rec_cross_b': (0.0, 0.8)}
    factors = {'L0_rec_b1': 27.041, 'L0_rec_b2': 8.0, 'L0_rec_b3': 8.0, 'L0_rec_b4': 4.327}
    for name, (base, spread) in spreads.items():
        noise = np.random.default_rng([zlib.crc32(name.encode()), seed]).standard_normal(out[name].shape)
        drawn = base * np.exp(spread * noise) if base else spread * noise
        out[name] = jnp.asarray(drawn.astype(out[name].dtype))
    for name, factor in factors.items():
        out[name] = (out[name] * factor).astype(out[name].dtype)
    return out
```

```python
from contextlib import ExitStack

import concourse.bass as bass
from concourse import mybir
from concourse.alu_op_type import AluOpType as ALU

ACT = mybir.ActivationFunctionType
F32 = mybir.dt.float32
F32R = mybir.dt.float32r

P = 128
N = 512
SQUARES = 8
TILES_PER_QUAD = 4
STAGES = 2
RELUS = 2
BANKS = 4
SUM_STEPS = 5
PREP_STEPS = 3


class Layer:

    def __init__(self, k, out, first_tile, first_chunk, source, target, banks):
        self.k, self.out = k, out
        self.first_tile, self.first_chunk = first_tile, first_chunk
        self.source, self.target, self.banks = source, target, banks
        self.chunks_per_quad = TILES_PER_QUAD * SQUARES // k
        self.quads = out // self.chunks_per_quad
        self.tiles = self.quads * TILES_PER_QUAD

    def finished_in(self, j):
        return [c for c in range(self.chunks_per_quad) if ((c + 1) * self.k - 1) // SQUARES == j]


def build(nc, x, w_tiles, columns, out_bias, out, widths):
    blocks = x.shape[0]
    k_in, *outs = [w // P for w in widths]

    with ExitStack() as ctx:
        def sb(name, shape, dt=F32):
            return ctx.enter_context(nc.sbuf_tensor(name, shape, dt))

        def sem(name):
            return ctx.enter_context(nc.semaphore(name))

        feat_hi, feat_lo = sb("feat_hi", [P, k_in, N], F32R), sb("feat_lo", [P, k_in, N], F32R)
        odd_hi, odd_lo = sb("odd_hi", [P, outs[0], N], F32R), sb("odd_lo", [P, outs[0], N], F32R)
        even_hi, even_lo = sb("even_hi", [P, outs[1], N], F32R), sb("even_lo", [P, outs[1], N], F32R)
        stage = sb("stage", [P, STAGES, SQUARES * P])
        w_hi = sb("w_hi", [P, TILES_PER_QUAD, SQUARES * P], F32R)
        w_lo = sb("w_lo", [P, TILES_PER_QUAD, SQUARES * P], F32R)
        x_raw = sb("x_raw", [P, k_in, N])
        x_tmp = sb("x_tmp", [P, N])
        relu = sb("relu", [P, RELUS, N])
        acc = sb("acc", [P, N])
        acc_hi, acc_lo = sb("acc_hi", [P, N], F32R), sb("acc_lo", [P, N], F32R)
        out_row = sb("out_row", [1, N])
        cols = sb("cols", [P, columns.shape[1]])
        bias_out = sb("bias_out", [1, 1])
        ones = sb("ones", [P, P], F32R)
        bank = [ctx.enter_context(nc.psum_tensor(f"bank{i}", [P, N], F32)) for i in range(8)]
        x_sum, out_sum = bank[6], bank[7]

        n_bias = sum(outs)
        cross_w, cross_b, w_out = n_bias, n_bias + k_in, n_bias + 2 * k_in

        layers, tile, chunk = [], 0, 0
        for k, o, source, target, banks in (
            (k_in, outs[0], (feat_hi, feat_lo), (odd_hi, odd_lo), bank[0:BANKS]),
            (outs[0], outs[1], (odd_hi, odd_lo), (even_hi, even_lo), bank[4:6]),
            (outs[1], outs[2], (even_hi, even_lo), (odd_hi, odd_lo), bank[4:6]),
            (outs[2], outs[3], (odd_hi, odd_lo), None, bank[0:BANKS]),
        ):
            layers.append(Layer(k, o, tile, chunk, source, target, banks))
            tile, chunk = tile + layers[-1].tiles, chunk + o
        tiles, chunks = tile, chunk
        assert tiles == w_tiles.shape[0] and layers[3].quads == 1
        assert layers[2].quads == k_in

        cols_loaded = sem("cols_loaded")
        x_loaded = sem("x_loaded")
        stage_loaded = [sem(f"stage{i}_loaded") for i in range(STAGES)]
        ones_set = sem("ones_set")
        w_hi_done = sem("w_hi_done")
        w_split = sem("w_split")
        tile_done = sem("tile_done")
        evacuated = sem("evacuated")
        chunk_ready = sem("chunk_ready")
        sum_step = sem("sum_step")
        x_acc_ready = sem("x_acc_ready")
        x_summed = sem("x_summed")
        prep_step = sem("prep_step")
        feat_ready = sem("feat_ready")
        out_hi_done = sem("out_hi_done")
        out_acc_ready = sem("out_acc_ready")
        out_summed = sem("out_summed")
        out_row_ready = sem("out_row_ready")
        out_row_free = sem("out_row_free")

        block = ctx.enter_context(nc.Block())

        def row_blocks(eng, body):
            body(0, False, True)
            with eng.Fori(1, blocks - 1) as b:
                body(b, True, True)
            body(blocks - 1, True, False)

        def quads(eng, layer, body):
            if layer.quads == 1:
                return body(0)
            with eng.Fori(0, layer.quads) as q:
                body(q)

        @block.gpsimd
        def _(pool):
            nc.gpsimd.memset(ones[:].bitcast(F32), 1.0).then_inc(ones_set, 1)
            pool.sem_inc(w_split, STAGES)
            pool.sem_inc(evacuated, BANKS)
            pool.sem_inc(chunk_ready, RELUS)
            pool.sem_inc(out_row_free, 16)

        @block.sync
        def _(sp):
            def load_pair(b, pair):
                for s in range(STAGES):
                    t = b * tiles + pair * STAGES + s
                    sp.wait_ge(w_split, t + 1)
                    sp.dma_start(stage[:, s, :], w_tiles[bass.ds(pair * STAGES + s, 1), :, :]
                                 .rearrange("t p n -> (t p) n")).then_inc(stage_loaded[s], 16)

            def row_block(b, has_prev, has_next):
                after_first = layers[0].tiles // STAGES
                after_second = after_first + layers[1].tiles // STAGES
                with sp.Fori(0, after_first) as pair:
                    load_pair(b, pair)
                if has_next:
                    sp.wait_ge(feat_ready, (b + 1) * k_in)
                    sp.dma_start(x_raw[:], x[bass.ds(b + 1, 1)].rearrange("b p k n -> (b p) k n")).then_inc(x_loaded, 16)
                with sp.Fori(after_first, after_second) as pair:
                    load_pair(b, pair)
                if has_prev:
                    store_row(b - 1)
                with sp.Fori(after_second, tiles // STAGES) as pair:
                    load_pair(b, pair)

            def store_row(b):
                sp.wait_ge(out_row_ready, b + 1)
                sp.dma_start(out[bass.ds(b, 1), :], out_row[:]).then_inc(out_row_free, 16)

            sp.dma_start(x_raw[:], x[0]).then_inc(x_loaded, 16)
            sp.dma_start(cols[:], columns).then_inc(cols_loaded, 16)
            sp.dma_start(bias_out[:], out_bias).then_inc(cols_loaded, 16)
            row_blocks(sp, row_block)
            store_row(blocks - 1)
            sp.wait_ge(out_row_free, 16 + 16 * blocks)

        @block.scalar
        def _(act):
            def split_hi(t, slot):
                act.wait_ge(stage_loaded[slot % STAGES], (t - slot) * (16 // STAGES) + 16 * (slot // STAGES + 1))
                nc.scalar.activation(w_hi[:, slot, :], stage[:, slot % STAGES, :], ACT.Copy).then_inc(w_hi_done, 1)

            def quad(layer, b, q, ahead):
                t0 = b * tiles + layer.first_tile + q * TILES_PER_QUAD
                for j in range(TILES_PER_QUAD):
                    act.wait_ge(tile_done, t0 + j + 1)
                    for c in layer.finished_in(j):
                        in_block = layer.first_chunk + q * layer.chunks_per_quad + c
                        source = layer.banks[c % len(layer.banks)]
                        bias = cols[:, bass.ds(in_block, 1)]
                        act.wait_ge(chunk_ready, b * chunks + in_block + 1)
                        step = nc.scalar.activation(relu[:, c % RELUS, :], source[:], ACT.Relu, bias=bias)
                        if layer.target:
                            at = bass.ds(q * layer.chunks_per_quad + c, 1)
                            step = nc.scalar.activation(layer.target[0][:, at, :].rearrange("p a n -> p (a n)"),
                                                        source[:], ACT.Relu, bias=bias)
                        step.then_inc(evacuated, 1)
                    if ahead:
                        split_hi(t0 + j + TILES_PER_QUAD, j)

            def row_block(b, has_prev, has_next):
                for layer in layers:
                    quads(act, layer, lambda q, layer=layer: quad(layer, b, q, has_next or layer is not layers[3]))

            for slot in range(TILES_PER_QUAD):
                split_hi(slot, slot)
            act.wait_ge(cols_loaded, 32)
            row_blocks(act, row_block)

        @block.vector
        def _(dve):
            def split_lo(t, slot):
                dve.wait_ge(w_hi_done, t + 1)
                nc.vector.tensor_tensor(w_lo[:, slot, :], stage[:, slot % STAGES, :],
                                        w_hi[:, slot, :].bitcast(F32), ALU.subtract).then_inc(w_split, 1)

            def quad(layer, b, q, ahead):
                t0 = b * tiles + layer.first_tile + q * TILES_PER_QUAD
                for j in range(TILES_PER_QUAD):
                    for c in layer.finished_in(j):
                        n = b * chunks + layer.first_chunk + q * layer.chunks_per_quad + c
                        dve.wait_ge(evacuated, BANKS + n + 1)
                        r = relu[:, c % RELUS, :]
                        if layer.target:
                            hi, lo = [t[:, bass.ds(q * layer.chunks_per_quad + c, 1), :].rearrange("p a n -> p (a n)")
                                      for t in layer.target]
                            nc.vector.tensor_tensor(lo, r, hi.bitcast(F32), ALU.subtract).then_inc(chunk_ready, 1)
                        elif c == 0:
                            nc.vector.tensor_scalar(acc[:], r, cols[:, w_out:w_out + 1], None, ALU.mult)\
                                .then_inc(chunk_ready, 1)
                        else:
                            dve.wait_ge(chunk_ready, RELUS + n)
                            nc.vector.scalar_tensor_tensor(acc[:], r, cols[:, w_out + c:w_out + c + 1], acc[:],
                                                           ALU.mult, ALU.add).then_inc(chunk_ready, 1)
                    if ahead:
                        split_lo(t0 + j + TILES_PER_QUAD, j)

            def sum_cross(b):
                dve.wait_ge(x_loaded, (b + 1) * 16)
                for k in range(k_in):
                    w = cols[:, cross_w + k:cross_w + k + 1]
                    if k == 0:
                        step = nc.vector.tensor_scalar(acc[:], x_raw[:, k, :], w, None, ALU.mult)
                    else:
                        dve.wait_ge(sum_step, b * SUM_STEPS + k)
                        step = nc.vector.scalar_tensor_tensor(acc[:], x_raw[:, k, :], w, acc[:], ALU.mult, ALU.add)
                    step.then_inc(sum_step, 1)
                dve.wait_ge(sum_step, b * SUM_STEPS + k_in)
                nc.vector.tensor_copy(acc_hi[:], acc[:]).then_inc(sum_step, 1)
                dve.wait_ge(sum_step, (b + 1) * SUM_STEPS)
                nc.vector.tensor_tensor(acc_lo[:], acc[:], acc_hi[:].bitcast(F32), ALU.subtract)\
                    .then_inc(x_acc_ready, 1)

            def prepare_feature(b, k):
                n = (b * k_in + k) * PREP_STEPS
                raw = x_raw[:, bass.ds(k, 1), :].rearrange("p a n -> p (a n)")
                hi, lo = [t[:, bass.ds(k, 1), :].rearrange("p a n -> p (a n)") for t in (feat_hi, feat_lo)]
                dve.wait_ge(x_summed, b + 1)
                nc.vector.tensor_tensor(x_tmp[:], x_sum[:], raw, ALU.mult).then_inc(prep_step, 1)
                dve.wait_ge(prep_step, n + 1)
                nc.vector.scalar_tensor_tensor(raw, x_tmp[:], cols[:, bass.ds(k + cross_b, 1)], raw,
                                               ALU.add, ALU.add).then_inc(prep_step, 1)
                dve.wait_ge(prep_step, n + 2)
                nc.vector.tensor_copy(hi, raw).then_inc(prep_step, 1)
                dve.wait_ge(prep_step, n + 3)
                nc.vector.tensor_tensor(lo, raw, hi.bitcast(F32), ALU.subtract).then_inc(feat_ready, 1)

            def split_out(b):
                dve.wait_ge(chunk_ready, RELUS + (b + 1) * chunks)
                nc.vector.tensor_copy(acc_hi[:], acc[:]).then_inc(out_hi_done, 1)
                dve.wait_ge(out_hi_done, b + 1)
                nc.vector.tensor_tensor(acc_lo[:], acc[:], acc_hi[:].bitcast(F32), ALU.subtract)\
                    .then_inc(out_acc_ready, 1)

            def finish_row(b):
                dve.wait_ge(out_summed, b + 1)
                dve.wait_ge(out_row_free, (b + 1) * 16)
                nc.vector.tensor_scalar(out_row[:], out_sum[0:1, :], bias_out[:], None, ALU.add)\
                    .then_inc(out_row_ready, 1)

            def row_block(b, has_prev, has_next):
                quads(dve, layers[0], lambda q: quad(layers[0], b, q, True))
                if has_prev:
                    finish_row(b - 1)
                if has_next:
                    sum_cross(b + 1)
                quads(dve, layers[1], lambda q: quad(layers[1], b, q, True))

                def third(q):
                    quad(layers[2], b, q, True)
                    if has_next:
                        prepare_feature(b + 1, q)

                quads(dve, layers[2], third)
                quads(dve, layers[3], lambda q: quad(layers[3], b, q, has_next))
                split_out(b)

            dve.wait_ge(cols_loaded, 32)
            sum_cross(0)
            for slot in range(TILES_PER_QUAD):
                split_lo(slot, slot)
                prepare_feature(0, slot)
            row_blocks(dve, row_block)
            finish_row(blocks - 1)

        @block.tensor
        def _(pe):
            def quad(layer, b, q):
                t0 = b * tiles + layer.first_tile + q * TILES_PER_QUAD
                hi, lo = layer.source
                for square in range(TILES_PER_QUAD * SQUARES):
                    slot, at = divmod(square, SQUARES)
                    c, k = divmod(square, layer.k)
                    n = b * chunks + layer.first_chunk + q * layer.chunks_per_quad + c
                    if at == 0:
                        pe.wait_ge(w_split, STAGES + t0 + slot + 1)
                    if k == 0:
                        pe.wait_ge(evacuated, BANKS + n + 1 - len(layer.banks))
                    if c == 0 and layer is layers[0]:
                        pe.wait_ge(feat_ready, b * k_in + k + 1)
                    elif c == 0:
                        pe.wait_ge(chunk_ready, RELUS + b * chunks + layer.first_chunk - layer.k + k + 1)
                    target = layer.banks[c % len(layer.banks)]
                    wh, wl = [w[:, slot, at * P:(at + 1) * P] for w in (w_hi, w_lo)]
                    nc.tensor.matmul(target[:], wh, hi[:, k, :], start=k == 0, stop=False)
                    nc.tensor.matmul(target[:], wh, lo[:, k, :], start=False, stop=False)
                    last = nc.tensor.matmul(target[:], wl, hi[:, k, :], start=False, stop=k == layer.k - 1)
                    if at == SQUARES - 1:
                        last.then_inc(tile_done, 1)

            def sum_partitions(target):
                nc.tensor.matmul(target[:], ones[:], acc_hi[:], start=True, stop=False)
                return nc.tensor.matmul(target[:], ones[:], acc_lo[:], start=False, stop=True)

            def sum_cross(b):
                pe.wait_ge(x_acc_ready, b + 1)
                sum_partitions(x_sum).then_inc(x_summed, 1)

            def sum_out(b):
                pe.wait_ge(out_acc_ready, b + 1)
                sum_partitions(out_sum).then_inc(out_summed, 1)

            def row_block(b, has_prev, has_next):
                for i, layer in enumerate(layers):
                    quads(pe, layer, lambda q: quad(layer, b, q))
                    if i == 0 and has_prev:
                        sum_out(b - 1)
                    if i == 1 and has_next:
                        sum_cross(b + 1)

            pe.wait_ge(ones_set, 1)
            sum_cross(0)
            row_blocks(pe, row_block)
            sum_out(blocks - 1)


def kernel(r_x, L0_rec_cross_w, L0_rec_cross_b, L0_rec_W1, L0_rec_b1, L0_rec_W2, L0_rec_b2,
           L0_rec_W3, L0_rec_b3, L0_rec_W4, L0_rec_b4, L0_rec_Wo, L0_rec_bo):
    import numpy as np
    import concourse.bacc as bacc
    from concourse.bass_utils import run_bass_kernel_spmd

    def squares(w):
        w = np.asarray(w)
        return w.reshape(w.shape[0] // P, P, w.shape[1] // P, P).transpose(0, 2, 3, 1).reshape(-1, P, P)

    def by_partition(v):
        return np.asarray(v).reshape(-1, P).T

    x = np.asarray(r_x)
    rows, features = x.shape
    weights = (L0_rec_W1, L0_rec_W2, L0_rec_W3, L0_rec_W4)
    tiles = np.concatenate([squares(w) for w in weights]).reshape(-1, SQUARES, P, P).transpose(0, 2, 1, 3)
    arrays = {
        "x": np.ascontiguousarray(x.reshape(rows // N, N, features // P, P).transpose(0, 3, 2, 1)),
        "w_tiles": np.ascontiguousarray(tiles.reshape(-1, P, SQUARES * P)),
        "columns": np.ascontiguousarray(np.concatenate(
            [by_partition(v) for v in (L0_rec_b1, L0_rec_b2, L0_rec_b3, L0_rec_b4,
                                       L0_rec_cross_w, L0_rec_cross_b, L0_rec_Wo)], axis=1)),
        "out_bias": np.asarray(L0_rec_bo).reshape(1, 1),
    }
    nc = bacc.Bacc("TRN2", target_bir_lowering=False, num_devices=1)
    aps = [nc.dram_tensor(name, a.shape, mybir.dt.from_np(a.dtype), kind="ExternalInput").ap()
           for name, a in arrays.items()]
    out = nc.dram_tensor("out", (rows // N, N), F32, kind="ExternalOutput").ap()
    build(nc, *aps, out, [features, *(np.shape(w)[0] for w in weights)])
    result = run_bass_kernel_spmd(nc, [arrays], core_ids=[0])
    return result.results[0]["out"].reshape(rows, 1)
```

```python
from contextlib import ExitStack

import concourse.bass as bass
from concourse import mybir
from concourse.alu_op_type import AluOpType as ALU

ACT = mybir.ActivationFunctionType
F32 = mybir.dt.float32
F32R = mybir.dt.float32r

P = 128
N = 512
SQUARES = 8
TILES_PER_QUAD = 4
STAGES = 2
RELUS = 2
BANKS = 4
SUM_STEPS = 5
PREP_STEPS = 3


class Layer:

    def __init__(self, k, out, first_tile, first_chunk, source, target):
        self.k = k
        self.first_tile, self.first_chunk = first_tile, first_chunk
        self.source, self.target = source, target
        self.chunks_per_quad = TILES_PER_QUAD * SQUARES // k
        self.quads = out // self.chunks_per_quad
        self.tiles = self.quads * TILES_PER_QUAD
        self.unroll = max(1, BANKS // self.chunks_per_quad)

    def finished_in(self, j):
        return [c for c in range(self.chunks_per_quad) if ((c + 1) * self.k - 1) // SQUARES == j]


def build(nc, x, w_tiles, columns, out_bias, out, widths):
    blocks = x.shape[0]
    k_in, *outs = [w // P for w in widths]

    with ExitStack() as ctx:
        def sb(name, shape, dt=F32):
            return ctx.enter_context(nc.sbuf_tensor(name, shape, dt))

        def sem(name):
            return ctx.enter_context(nc.semaphore(name))

        feat_hi, feat_lo = sb("feat_hi", [P, k_in, N], F32R), sb("feat_lo", [P, k_in, N], F32R)
        odd_hi, odd_lo = sb("odd_hi", [P, outs[0], N], F32R), sb("odd_lo", [P, outs[0], N], F32R)
        even_hi, even_lo = sb("even_hi", [P, outs[1], N], F32R), sb("even_lo", [P, outs[1], N], F32R)
        stage = sb("stage", [P, STAGES, SQUARES * P])
        w_hi = sb("w_hi", [P, TILES_PER_QUAD, SQUARES * P], F32R)
        w_lo = sb("w_lo", [P, TILES_PER_QUAD, SQUARES * P], F32R)
        x_raw = sb("x_raw", [P, k_in, N])
        x_tmp = sb("x_tmp", [P, N])
        relu = sb("relu", [P, RELUS, N])
        acc = sb("acc", [P, N])
        acc_hi, acc_lo = sb("acc_hi", [P, N], F32R), sb("acc_lo", [P, N], F32R)
        out_row = sb("out_row", [1, N])
        cols = sb("cols", [P, columns.shape[1]])
        bias_out = sb("bias_out", [1, 1])
        ones = sb("ones", [P, P], F32R)
        bank = [ctx.enter_context(nc.psum_tensor(f"bank{i}", [P, N], F32)) for i in range(BANKS + 2)]
        x_sum, out_sum = bank[BANKS], bank[BANKS + 1]

        n_bias = sum(outs)
        cross_w, cross_b, w_out = n_bias, n_bias + k_in, n_bias + 2 * k_in

        layers, tile, chunk = [], 0, 0
        for k, o, source, target in (
            (k_in, outs[0], (feat_hi, feat_lo), (odd_hi, odd_lo)),
            (outs[0], outs[1], (odd_hi, odd_lo), (even_hi, even_lo)),
            (outs[1], outs[2], (even_hi, even_lo), (odd_hi, odd_lo)),
            (outs[2], outs[3], (odd_hi, odd_lo), None),
        ):
            layers.append(Layer(k, o, tile, chunk, source, target))
            assert chunk % BANKS == 0 and o % BANKS == 0
            tile, chunk = tile + layers[-1].tiles, chunk + o
        tiles, chunks = tile, chunk
        assert tiles == w_tiles.shape[0] and layers[3].quads == 1
        assert layers[2].quads == k_in

        cols_loaded, out_bias_loaded = sem("cols_loaded"), sem("out_bias_loaded")
        first_x_loaded = [sem(f"first_x{k}_loaded") for k in range(k_in)]
        x_loaded = sem("x_loaded")
        stage_loaded = [sem(f"stage{i}_loaded") for i in range(STAGES)]
        ones_set = sem("ones_set")
        w_hi_done = sem("w_hi_done")
        w_split = sem("w_split")
        tile_done = sem("tile_done")
        evacuated = sem("evacuated")
        chunk_ready = sem("chunk_ready")
        sum_step = sem("sum_step")
        x_acc_ready = sem("x_acc_ready")
        x_summed = sem("x_summed")
        first_product = sem("first_product")
        first_feature = sem("first_feature")
        first_feature_hi = sem("first_feature_hi")
        prep_step = sem("prep_step")
        feat_ready = sem("feat_ready")
        out_hi_done = sem("out_hi_done")
        out_acc_ready = sem("out_acc_ready")
        out_summed = sem("out_summed")
        out_row_ready = sem("out_row_ready")
        out_row_free = sem("out_row_free")

        block = ctx.enter_context(nc.Block())

        def row_blocks(eng, body):
            body(0, False, True)
            with eng.Fori(1, blocks - 1) as b:
                body(b, True, True)
            body(blocks - 1, True, False)

        def quads(eng, layer, body):
            if layer.quads == 1:
                return body(0, 0)
            with eng.Fori(0, layer.quads // layer.unroll) as i:
                for u in range(layer.unroll):
                    body(i * layer.unroll + u, u)

        @block.gpsimd
        def _(pool):
            nc.gpsimd.memset(ones[:].bitcast(F32), 1.0).then_inc(ones_set, 1)
            pool.sem_inc(w_split, STAGES)
            pool.sem_inc(evacuated, BANKS)
            pool.sem_inc(chunk_ready, RELUS)
            pool.sem_inc(out_row_free, 16)

        @block.sync
        def _(sp):
            def load_pair(b, pair):
                for s in range(STAGES):
                    t = b * tiles + pair * STAGES + s
                    sp.wait_ge(w_split, t + 1)
                    sp.dma_start(stage[:, s, :], w_tiles[bass.ds(pair * STAGES + s, 1), :, :]
                                 .rearrange("t p n -> (t p) n")).then_inc(stage_loaded[s], 16)

            def row_block(b, has_prev, has_next):
                after_first = layers[0].tiles // STAGES
                after_second = after_first + layers[1].tiles // STAGES
                with sp.Fori(0, after_first) as pair:
                    load_pair(b, pair)
                if has_next:
                    sp.wait_ge(feat_ready, (b + 1) * k_in)
                    sp.dma_start(x_raw[:], x[bass.ds(b + 1, 1)].rearrange("b p k n -> (b p) k n")).then_inc(x_loaded, 16)
                with sp.Fori(after_first, after_second) as pair:
                    load_pair(b, pair)
                if has_prev:
                    store_row(b - 1)
                with sp.Fori(after_second, tiles // STAGES) as pair:
                    load_pair(b, pair)

            def store_row(b):
                sp.wait_ge(out_row_ready, b + 1)
                sp.dma_start(out[bass.ds(b, 1), :], out_row[:]).then_inc(out_row_free, 16)

            sp.dma_start(cols[:], columns).then_inc(cols_loaded, 16)
            for k in range(k_in):
                sp.dma_start(x_raw[:, k, :], x[0, :, k, :]).then_inc(first_x_loaded[k], 16)
            sp.dma_start(bias_out[:], out_bias).then_inc(out_bias_loaded, 16)
            row_blocks(sp, row_block)
            store_row(blocks - 1)
            sp.wait_ge(out_row_free, 16 + 16 * blocks)

        @block.scalar
        def _(act):
            def split_hi(t, slot):
                act.wait_ge(stage_loaded[slot % STAGES], (t - slot) * (16 // STAGES) + 16 * (slot // STAGES + 1))
                nc.scalar.activation(w_hi[:, slot, :], stage[:, slot % STAGES, :], ACT.Copy).then_inc(w_hi_done, 1)

            def quad(layer, b, q, u, ahead):
                t0 = b * tiles + layer.first_tile + q * TILES_PER_QUAD
                for j in range(TILES_PER_QUAD):
                    act.wait_ge(tile_done, t0 + j + 1)
                    for c in layer.finished_in(j):
                        in_block = layer.first_chunk + q * layer.chunks_per_quad + c
                        source = bank[(u * layer.chunks_per_quad + c) % BANKS]
                        bias = cols[:, bass.ds(in_block, 1)]
                        act.wait_ge(chunk_ready, b * chunks + in_block + 1)
                        step = nc.scalar.activation(relu[:, c % RELUS, :], source[:], ACT.Relu, bias=bias)
                        if layer.target:
                            at = bass.ds(q * layer.chunks_per_quad + c, 1)
                            step = nc.scalar.activation(layer.target[0][:, at, :].rearrange("p a n -> p (a n)"),
                                                        source[:], ACT.Relu, bias=bias)
                        step.then_inc(evacuated, 1)
                    if ahead:
                        split_hi(t0 + j + TILES_PER_QUAD, j)

            def row_block(b, has_prev, has_next):
                for layer in layers:
                    ahead = has_next or layer is not layers[3]
                    quads(act, layer, lambda q, u: quad(layer, b, q, u, ahead))

            split_hi(0, 0)
            split_hi(1, 1)
            for k in range(k_in):
                act.wait_ge(first_feature, k + 1)
                nc.scalar.activation(feat_hi[:, k, :], x_raw[:, k, :], ACT.Copy).then_inc(first_feature_hi, 1)
            split_hi(2, 2)
            split_hi(3, 3)
            act.wait_ge(cols_loaded, 16)
            row_blocks(act, row_block)

        @block.vector
        def _(dve):
            def split_lo(t, slot):
                dve.wait_ge(w_hi_done, t + 1)
                nc.vector.tensor_tensor(w_lo[:, slot, :], stage[:, slot % STAGES, :],
                                        w_hi[:, slot, :].bitcast(F32), ALU.subtract).then_inc(w_split, 1)

            def quad(layer, b, q, ahead):
                t0 = b * tiles + layer.first_tile + q * TILES_PER_QUAD
                for j in range(TILES_PER_QUAD):
                    for c in layer.finished_in(j):
                        n = b * chunks + layer.first_chunk + q * layer.chunks_per_quad + c
                        dve.wait_ge(evacuated, BANKS + n + 1)
                        r = relu[:, c % RELUS, :]
                        if layer.target:
                            hi, lo = [t[:, bass.ds(q * layer.chunks_per_quad + c, 1), :].rearrange("p a n -> p (a n)")
                                      for t in layer.target]
                            nc.vector.tensor_tensor(lo, r, hi.bitcast(F32), ALU.subtract).then_inc(chunk_ready, 1)
                        elif c == 0:
                            nc.vector.tensor_scalar(acc[:], r, cols[:, w_out:w_out + 1], None, ALU.mult)\
                                .then_inc(chunk_ready, 1)
                        else:
                            dve.wait_ge(chunk_ready, RELUS + n)
                            nc.vector.scalar_tensor_tensor(acc[:], r, cols[:, w_out + c:w_out + c + 1], acc[:],
                                                           ALU.mult, ALU.add).then_inc(chunk_ready, 1)
                    if ahead:
                        split_lo(t0 + j + TILES_PER_QUAD, j)

            def sum_cross(b, by_chunk=False):
                if not by_chunk:
                    dve.wait_ge(x_loaded, b * 16)
                for k in range(k_in):
                    if by_chunk:
                        dve.wait_ge(first_x_loaded[k], 16)
                    w = cols[:, cross_w + k:cross_w + k + 1]
                    if k == 0:
                        step = nc.vector.tensor_scalar(acc[:], x_raw[:, k, :], w, None, ALU.mult)
                    else:
                        dve.wait_ge(sum_step, b * SUM_STEPS + k)
                        step = nc.vector.scalar_tensor_tensor(acc[:], x_raw[:, k, :], w, acc[:], ALU.mult, ALU.add)
                    step.then_inc(sum_step, 1)
                dve.wait_ge(sum_step, b * SUM_STEPS + k_in)
                nc.vector.tensor_copy(acc_hi[:], acc[:]).then_inc(sum_step, 1)
                dve.wait_ge(sum_step, (b + 1) * SUM_STEPS)
                nc.vector.tensor_tensor(acc_lo[:], acc[:], acc_hi[:].bitcast(F32), ALU.subtract)\
                    .then_inc(x_acc_ready, 1)

            def prepare_feature(b, k):
                n = ((b - 1) * k_in + k) * PREP_STEPS
                raw = x_raw[:, bass.ds(k, 1), :].rearrange("p a n -> p (a n)")
                hi, lo = [t[:, bass.ds(k, 1), :].rearrange("p a n -> p (a n)") for t in (feat_hi, feat_lo)]
                dve.wait_ge(x_summed, b + 1)
                nc.vector.tensor_tensor(x_tmp[:], x_sum[:], raw, ALU.mult).then_inc(prep_step, 1)
                dve.wait_ge(prep_step, n + 1)
                nc.vector.scalar_tensor_tensor(raw, x_tmp[:], cols[:, bass.ds(k + cross_b, 1)], raw,
                                               ALU.add, ALU.add).then_inc(prep_step, 1)
                dve.wait_ge(prep_step, n + 2)
                nc.vector.tensor_copy(hi, raw).then_inc(prep_step, 1)
                dve.wait_ge(prep_step, n + 3)
                nc.vector.tensor_tensor(lo, raw, hi.bitcast(F32), ALU.subtract).then_inc(feat_ready, 1)

            def prepare_first_features():
                products = [relu[:, 0, :], relu[:, 1, :], x_tmp[:], acc[:]]
                assert len(products) == k_in
                for step in range(k_in + 2):
                    if step < k_in:
                        if step == 0:
                            dve.wait_ge(x_summed, 1)
                        nc.vector.tensor_tensor(products[step], x_sum[:], x_raw[:, step, :], ALU.mult)\
                            .then_inc(first_product, 1)
                    if 0 <= (k := step - 1) < k_in:
                        dve.wait_ge(first_product, k + 1)
                        nc.vector.scalar_tensor_tensor(
                            x_raw[:, k, :], products[k], cols[:, cross_b + k:cross_b + k + 1],
                            x_raw[:, k, :], ALU.add, ALU.add).then_inc(first_feature, 1)
                    if (k := step - 2) >= 0:
                        dve.wait_ge(first_feature_hi, k + 1)
                        nc.vector.tensor_tensor(feat_lo[:, k, :], x_raw[:, k, :], feat_hi[:, k, :].bitcast(F32),
                                                ALU.subtract).then_inc(feat_ready, 1)

            def split_out(b):
                dve.wait_ge(chunk_ready, RELUS + (b + 1) * chunks)
                nc.vector.tensor_copy(acc_hi[:], acc[:]).then_inc(out_hi_done, 1)
                dve.wait_ge(out_hi_done, b + 1)
                nc.vector.tensor_tensor(acc_lo[:], acc[:], acc_hi[:].bitcast(F32), ALU.subtract)\
                    .then_inc(out_acc_ready, 1)

            def finish_row(b):
                dve.wait_ge(out_bias_loaded, 16)
                dve.wait_ge(out_summed, b + 1)
                dve.wait_ge(out_row_free, (b + 1) * 16)
                nc.vector.tensor_scalar(out_row[:], out_sum[0:1, :], bias_out[:], None, ALU.add)\
                    .then_inc(out_row_ready, 1)

            def row_block(b, has_prev, has_next):
                quads(dve, layers[0], lambda q, _: quad(layers[0], b, q, True))
                if has_prev:
                    finish_row(b - 1)
                if has_next:
                    sum_cross(b + 1)
                quads(dve, layers[1], lambda q, _: quad(layers[1], b, q, True))

                def third(q, _):
                    quad(layers[2], b, q, True)
                    if has_next:
                        prepare_feature(b + 1, q)

                quads(dve, layers[2], third)
                quads(dve, layers[3], lambda q, _: quad(layers[3], b, q, has_next))
                split_out(b)

            dve.wait_ge(cols_loaded, 16)
            sum_cross(0, by_chunk=True)
            split_lo(0, 0)
            prepare_first_features()
            for slot in range(1, TILES_PER_QUAD):
                split_lo(slot, slot)
            row_blocks(dve, row_block)
            finish_row(blocks - 1)

        @block.tensor
        def _(pe):
            def quad(layer, b, q, u):
                t0 = b * tiles + layer.first_tile + q * TILES_PER_QUAD
                hi, lo = layer.source
                for square in range(TILES_PER_QUAD * SQUARES):
                    slot, at = divmod(square, SQUARES)
                    c, k = divmod(square, layer.k)
                    n = b * chunks + layer.first_chunk + q * layer.chunks_per_quad + c
                    if at == 0:
                        pe.wait_ge(w_split, STAGES + t0 + slot + 1)
                    if k == 0:
                        pe.wait_ge(evacuated, n + 1)
                    if (u, c) != (0, 0):
                        pass
                    elif layer is layers[0]:
                        pe.wait_ge(feat_ready, b * k_in + k + 1)
                    else:
                        pe.wait_ge(chunk_ready, RELUS + b * chunks + layer.first_chunk - layer.k + k + 1)
                    target = bank[(u * layer.chunks_per_quad + c) % BANKS]
                    wh, wl = [w[:, slot, at * P:(at + 1) * P] for w in (w_hi, w_lo)]
                    nc.tensor.matmul(target[:], wh, hi[:, k, :], start=k == 0, stop=False)
                    nc.tensor.matmul(target[:], wh, lo[:, k, :], start=False, stop=False)
                    last = nc.tensor.matmul(target[:], wl, hi[:, k, :], start=False, stop=k == layer.k - 1)
                    if at == SQUARES - 1:
                        last.then_inc(tile_done, 1)

            def sum_partitions(target):
                nc.tensor.matmul(target[:], ones[:], acc_hi[:], start=True, stop=False)
                return nc.tensor.matmul(target[:], ones[:], acc_lo[:], start=False, stop=True)

            def sum_cross(b):
                pe.wait_ge(x_acc_ready, b + 1)
                sum_partitions(x_sum).then_inc(x_summed, 1)

            def sum_out(b):
                pe.wait_ge(out_acc_ready, b + 1)
                sum_partitions(out_sum).then_inc(out_summed, 1)

            def row_block(b, has_prev, has_next):
                for i, layer in enumerate(layers):
                    quads(pe, layer, lambda q, u: quad(layer, b, q, u))
                    if i == 0 and has_prev:
                        sum_out(b - 1)
                    if i == 1 and has_next:
                        sum_cross(b + 1)

            pe.wait_ge(ones_set, 1)
            sum_cross(0)
            row_blocks(pe, row_block)
            sum_out(blocks - 1)


def kernel(r_x, L0_rec_cross_w, L0_rec_cross_b, L0_rec_W1, L0_rec_b1, L0_rec_W2, L0_rec_b2,
           L0_rec_W3, L0_rec_b3, L0_rec_W4, L0_rec_b4, L0_rec_Wo, L0_rec_bo):
    import numpy as np
    import concourse.bacc as bacc
    from concourse.bass_utils import run_bass_kernel_spmd

    def squares(w):
        w = np.asarray(w)
        return w.reshape(w.shape[0] // P, P, w.shape[1] // P, P).transpose(0, 2, 3, 1).reshape(-1, P, P)

    def by_partition(v):
        return np.asarray(v).reshape(-1, P).T

    x = np.asarray(r_x)
    rows, features = x.shape
    weights = (L0_rec_W1, L0_rec_W2, L0_rec_W3, L0_rec_W4)
    tiles = np.concatenate([squares(w) for w in weights]).reshape(-1, SQUARES, P, P).transpose(0, 2, 1, 3)
    arrays = {
        "x": np.ascontiguousarray(x.reshape(rows // N, N, features // P, P).transpose(0, 3, 2, 1)),
        "w_tiles": np.ascontiguousarray(tiles.reshape(-1, P, SQUARES * P)),
        "columns": np.ascontiguousarray(np.concatenate(
            [by_partition(v) for v in (L0_rec_b1, L0_rec_b2, L0_rec_b3, L0_rec_b4,
                                       L0_rec_cross_w, L0_rec_cross_b, L0_rec_Wo)], axis=1)),
        "out_bias": np.asarray(L0_rec_bo).reshape(1, 1),
    }
    nc = bacc.Bacc("TRN2", target_bir_lowering=False, num_devices=1)
    aps = [nc.dram_tensor(name, a.shape, mybir.dt.from_np(a.dtype), kind="ExternalInput").ap()
           for name, a in arrays.items()]
    out = nc.dram_tensor("out", (rows // N, N), F32, kind="ExternalOutput").ap()
    build(nc, *aps, out, [features, *(np.shape(w)[0] for w in weights)])
    result = run_bass_kernel_spmd(nc, [arrays], core_ids=[0])
    return result.results[0]["out"].reshape(rows, 1)
```
